# Optimizing a Trainium2 kernel written in Bass

```python
import numpy as np
import jax
import jax.numpy as jnp

def _softmax(x, axis=-1):
    return jax.nn.softmax(x, axis=axis)

def _gelu(x):
    return jax.nn.gelu(x, approximate=True)

def _silu(x):
    return jax.nn.silu(x)

def _sigmoid(x):
    return jax.nn.sigmoid(x)

def _layernorm(x, axis=-1, eps=1e-05):
    m = jnp.mean(x, axis=axis, keepdims=True)
    v = jnp.var(x, axis=axis, keepdims=True)
    return (x - m) / jnp.sqrt(v + eps)

def _scatter_add(tgt, idx, src, axis=0):
    return tgt.at[idx].add(src)

def _segment_sum(src, seg, n):
    return jax.ops.segment_sum(src, seg, n)
kernel_name = 'mk_xattn_ffn_d1_seqx_r4_e846c7'

def setup_inputs(seed: int=0):
    np.random.seed(seed)
    _w = jnp.asarray

    def _rec_inputs():
        import jax
        import jax.numpy as jnp
        _rk = jax.random.key(seed)
        x = 6.313e-05 + 0.9998 * jax.random.normal(jax.random.fold_in(_rk, 1), (8, 256, 256), jnp.float32)
        _lenS = 256 - jax.random.randint(jax.random.fold_in(_rk, 7), (8,), 0, max(1, 256 // 4) + 1, jnp.int32)
        _lenS2 = 120 - jax.random.randint(jax.random.fold_in(_rk, 8), (8,), 0, max(1, 120 // 4) + 1, jnp.int32)
        _ctx_1024P = jax.random.normal(jax.random.fold_in(_rk, 11), (8, 16, 256), jnp.float32)
        _ctx_1024c = jax.random.dirichlet(jax.random.fold_in(_rk, 511), 0.3 * jnp.ones((16,), jnp.float32), (8, 120))
        _ctx_1024t = jnp.einsum('bsk,bkd->bsd', _ctx_1024c, _ctx_1024P)
        _ctx_1024t = _ctx_1024t * jax.lax.rsqrt(jnp.mean(jnp.square(_ctx_1024t)) + 1e-12) * 0.953939
        ctx_1024 = -0.000214406 + 1.00034 * (_ctx_1024t + 0.3 * jax.random.normal(jax.random.fold_in(_rk, 611), (8, 120, 256), jnp.float32))
        return (x, ctx_1024)
    x, ctx_1024 = _rec_inputs()

    def _L0_xattn_setup():
        import jax, jax.numpy as jnp
        import numpy as np
        from jax import lax
        BIG = jnp.float32(1e+30)

        def _pairwise_euclidean(a, b):
            aa = jnp.sum(a * a, axis=-1)[:, None]
            bb = jnp.sum(b * b, axis=-1)[None, :]
            ab = a @ b.T
            return jnp.sqrt(jnp.maximum(aa + bb - 2.0 * ab, 0.0))

        def _dtw_cost(D):
            row0 = jnp.cumsum(D[0])

            def row_step(prev_row, d_row):
                first = d_row[0] + prev_row[0]

                def col_step(left, inp):
                    d_ij, up, diag = inp
                    r = d_ij + jnp.minimum(jnp.minimum(up, left), diag)
                    return (r, r)
                _, rest = lax.scan(col_step, first, (d_row[1:], prev_row[1:], prev_row[:-1]))
                row = jnp.concatenate([first[None], rest])
                return (row, row)
            _, rows = lax.scan(row_step, row0, D[1:])
            return jnp.concatenate([row0[None], rows], axis=0)

        def _backtrack(R, T1, T2):
            L = T1 + T2 - 1

            def step(carry, _):
                i, j, done = carry
                valid = jnp.logical_not(done)
                cd = jnp.where((i > 0) & (j > 0), R[jnp.maximum(i - 1, 0), jnp.maximum(j - 1, 0)], BIG)
                cu = jnp.where(i > 0, R[jnp.maximum(i - 1, 0), j], BIG)
                cl = jnp.where(j > 0, R[i, jnp.maximum(j - 1, 0)], BIG)
                choice = jnp.argmin(jnp.stack([cd, cu, cl]))
                ni = jnp.where(choice <= 1, i - 1, i)
                nj = jnp.where((choice == 0) | (choice == 2), j - 1, j)
                at_origin = (i == 0) & (j == 0)
                ni = jnp.where(at_origin, 0, ni)
                nj = jnp.where(at_origin, 0, nj)
                return ((ni, nj, done | at_origin), (i, j, valid))
            init = (jnp.int32(T1 - 1), jnp.int32(T2 - 1), jnp.bool_(False))
            _, (i_idx, j_idx, valid) = lax.scan(step, init, None, length=L)
            return (i_idx, j_idx, valid)

        def _align_one(small, large):
            T_small, d = small.shape
            T_large = large.shape[0]
            D = _pairwise_euclidean(small, large)
            R = _dtw_cost(D)
            i_idx, j_idx, valid = _backtrack(R, T_small, T_large)
            contrib = small[i_idx] * valid[:, None].astype(small.dtype)
            expanded = jnp.zeros((T_large, d), dtype=small.dtype).at[j_idx].add(contrib)
            return expanded
        key = jax.random.key(seed)
        k1, k2 = jax.random.split(key)
        teacher = jax.random.normal(k1, (16, 100, 256), dtype=jnp.float32)
        student = jax.random.normal(k2, (16, 150, 256), dtype=jnp.float32)
        return {'teacher_features': teacher, 'student_features': student}
    _L0_xattn_all = _L0_xattn_setup()
    _L0_xattn_in = {k: v for k, v in _L0_xattn_all.items() if k in ()}
    del _L0_xattn_all

    def _L0_ffn_setup():
        import jax, jax.numpy as jnp
        import numpy as np
        D_MODEL = 256
        N_HEADS = 16
        N_GROUPS = 4
        D_FF = 1024
        N_EXPERTS = 8
        TOP_K = 2
        BATCH = 2
        SEQ = 256
        D_K = D_MODEL // N_HEADS
        HPG = N_HEADS // N_GROUPS
        EPS = 1e-06

        def rms_norm(x, w):
            rms = jnp.sqrt(jnp.mean(x * x, axis=-1, keepdims=True) + EPS)
            return x / rms * w

        def rope(x):
            d = x.shape[-1]
            half = d // 2
            theta = 1.0 / 10000.0 ** (jnp.arange(half, dtype=jnp.float32) / half)
            pos = jnp.arange(x.shape[1], dtype=jnp.float32)[:, None]
            ang = pos * theta[None, :]
            cos, sin = (jnp.cos(ang), jnp.sin(ang))
            xe, xo = (x[..., 0::2], x[..., 1::2])
            return jnp.concatenate([xe * cos - xo * sin, xe * sin + xo * cos], axis=-1)

        def attention(x, Wq, Wk, Wv, Wo):
            B, S, _ = x.shape
            xr = rope(x)
            Q = (xr @ Wq).reshape(B, S, N_HEADS, D_K).transpose(0, 2, 1, 3)
            Q = Q.reshape(B, N_GROUPS, HPG, S, D_K)
            K = (xr @ Wk).reshape(B, S, N_GROUPS, D_K).transpose(0, 2, 1, 3)
            V = (xr @ Wv).reshape(B, S, N_GROUPS, D_K).transpose(0, 2, 1, 3)
            scores = jnp.einsum('bghsd,bgtd->bghst', Q, K) / jnp.sqrt(jnp.float32(D_K))
            mask = jnp.triu(jnp.full((S, S), -1000000000.0, dtype=scores.dtype), k=1)
            attn = jax.nn.softmax(scores + mask, axis=-1)
            out = jnp.einsum('bghst,bgtd->bghsd', attn, V)
            out = out.reshape(B, N_HEADS, S, D_K).transpose(0, 2, 1, 3).reshape(B, S, D_MODEL)
            return out @ Wo

        def moe(x, router_w, router_b, W1, b1, W2, b2, W3, b3):
            B, S, _ = x.shape
            logits = x @ router_w + router_b
            topv, topi = jax.lax.top_k(logits, TOP_K)
            topw = jax.nn.softmax(topv, axis=-1)
            onehot = jax.nn.one_hot(topi, N_EXPERTS, dtype=x.dtype)
            comb = jnp.einsum('bsk,bske->bse', topw, onehot)
            h1 = jnp.einsum('bsd,edf->ebsf', x, W1) + b1[:, None, None, :]
            h2 = jnp.einsum('bsd,edf->ebsf', x, W2) + b2[:, None, None, :]
            h = h2 * jax.nn.silu(h1)
            eo = jnp.einsum('ebsf,efd->ebsd', h, W3) + b3[:, None, None, :]
            return jnp.einsum('bse,ebsd->bsd', comb, eo)
        key = jax.random.key(seed)
        ks = jax.random.split(key, 16)
        s = 0.02
        return {'x': jax.random.normal(ks[0], (BATCH, SEQ, D_MODEL), dtype=jnp.float32), 'norm1_w': jnp.ones((D_MODEL,), jnp.float32), 'Wq': jax.random.normal(ks[1], (D_MODEL, D_MODEL), jnp.float32) * s, 'Wk': jax.random.normal(ks[2], (D_MODEL, N_GROUPS * D_K), jnp.float32) * s, 'Wv': jax.random.normal(ks[3], (D_MODEL, N_GROUPS * D_K), jnp.float32) * s, 'Wo': jax.random.normal(ks[4], (D_MODEL, D_MODEL), jnp.float32) * s, 'norm2_w': jnp.ones((D_MODEL,), jnp.float32), 'router_w': jax.random.normal(ks[5], (D_MODEL, N_EXPERTS), jnp.float32) * s, 'router_b': jnp.zeros((N_EXPERTS,), jnp.float32), 'W1': jax.random.normal(ks[6], (N_EXPERTS, D_MODEL, D_FF), jnp.float32) * s, 'b1': jnp.zeros((N_EXPERTS, D_FF), jnp.float32), 'W2': jax.random.normal(ks[7], (N_EXPERTS, D_MODEL, D_FF), jnp.float32) * s, 'b2': jnp.zeros((N_EXPERTS, D_FF), jnp.float32), 'W3': jax.random.normal(ks[8], (N_EXPERTS, D_FF, D_MODEL), jnp.float32) * s, 'b3': jnp.zeros((N_EXPERTS, D_MODEL), jnp.float32)}
    _L0_ffn_all = _L0_ffn_setup()
    _L0_ffn_in = {k: v for k, v in _L0_ffn_all.items() if k in ('norm1_w', 'Wq', 'Wk', 'Wv', 'Wo', 'norm2_w', 'router_w', 'router_b', 'W1', 'b1', 'W2', 'b2', 'W3', 'b3')}
    del _L0_ffn_all
    return {'x': x, 'ctx_1024': ctx_1024, 'L0_ffn_norm1_w': _L0_ffn_in['norm1_w'], 'L0_ffn_Wq': _L0_ffn_in['Wq'], 'L0_ffn_Wk': _L0_ffn_in['Wk'], 'L0_ffn_Wv': _L0_ffn_in['Wv'], 'L0_ffn_Wo': _L0_ffn_in['Wo'], 'L0_ffn_norm2_w': _L0_ffn_in['norm2_w'], 'L0_ffn_router_w': _L0_ffn_in['router_w'], 'L0_ffn_router_b': _L0_ffn_in['router_b'], 'L0_ffn_W1': _L0_ffn_in['W1'], 'L0_ffn_b1': _L0_ffn_in['b1'], 'L0_ffn_W2': _L0_ffn_in['W2'], 'L0_ffn_b2': _L0_ffn_in['b2'], 'L0_ffn_W3': _L0_ffn_in['W3'], 'L0_ffn_b3': _L0_ffn_in['b3']}

def reference(x, ctx_1024, L0_ffn_norm1_w, L0_ffn_Wq, L0_ffn_Wk, L0_ffn_Wv, L0_ffn_Wo, L0_ffn_norm2_w, L0_ffn_router_w, L0_ffn_router_b, L0_ffn_W1, L0_ffn_b1, L0_ffn_W2, L0_ffn_b2, L0_ffn_W3, L0_ffn_b3):
    import jax
    import jax.numpy as jnp

    def _L0_xattn_ref(teacher_features, student_features):
        import jax, jax.numpy as jnp
        import numpy as np
        from jax import lax
        BIG = jnp.float32(1e+30)

        def _pairwise_euclidean(a, b):
            aa = jnp.sum(a * a, axis=-1)[:, None]
            bb = jnp.sum(b * b, axis=-1)[None, :]
            ab = a @ b.T
            return jnp.sqrt(jnp.maximum(aa + bb - 2.0 * ab, 0.0))

        def _dtw_cost(D):
            row0 = jnp.cumsum(D[0])

            def row_step(prev_row, d_row):
                first = d_row[0] + prev_row[0]

                def col_step(left, inp):
                    d_ij, up, diag = inp
                    r = d_ij + jnp.minimum(jnp.minimum(up, left), diag)
                    return (r, r)
                _, rest = lax.scan(col_step, first, (d_row[1:], prev_row[1:], prev_row[:-1]))
                row = jnp.concatenate([first[None], rest])
                return (row, row)
            _, rows = lax.scan(row_step, row0, D[1:])
            return jnp.concatenate([row0[None], rows], axis=0)

        def _backtrack(R, T1, T2):
            L = T1 + T2 - 1

            def step(carry, _):
                i, j, done = carry
                valid = jnp.logical_not(done)
                cd = jnp.where((i > 0) & (j > 0), R[jnp.maximum(i - 1, 0), jnp.maximum(j - 1, 0)], BIG)
                cu = jnp.where(i > 0, R[jnp.maximum(i - 1, 0), j], BIG)
                cl = jnp.where(j > 0, R[i, jnp.maximum(j - 1, 0)], BIG)
                choice = jnp.argmin(jnp.stack([cd, cu, cl]))
                ni = jnp.where(choice <= 1, i - 1, i)
                nj = jnp.where((choice == 0) | (choice == 2), j - 1, j)
                at_origin = (i == 0) & (j == 0)
                ni = jnp.where(at_origin, 0, ni)
                nj = jnp.where(at_origin, 0, nj)
                return ((ni, nj, done | at_origin), (i, j, valid))
            init = (jnp.int32(T1 - 1), jnp.int32(T2 - 1), jnp.bool_(False))
            _, (i_idx, j_idx, valid) = lax.scan(step, init, None, length=L)
            return (i_idx, j_idx, valid)

        def _align_one(small, large):
            T_small, d = small.shape
            T_large = large.shape[0]
            D = _pairwise_euclidean(small, large)
            R = _dtw_cost(D)
            i_idx, j_idx, valid = _backtrack(R, T_small, T_large)
            contrib = small[i_idx] * valid[:, None].astype(small.dtype)
            expanded = jnp.zeros((T_large, d), dtype=small.dtype).at[j_idx].add(contrib)
            return expanded
        return jax.vmap(_align_one)(teacher_features, student_features)

    def _L0_ffn_ref(x, norm1_w, Wq, Wk, Wv, Wo, norm2_w, router_w, router_b, W1, b1, W2, b2, W3, b3):
        import jax, jax.numpy as jnp
        import numpy as np
        D_MODEL = 256
        N_HEADS = 16
        N_GROUPS = 4
        D_FF = 1024
        N_EXPERTS = 8
        TOP_K = 2
        BATCH = 2
        SEQ = 256
        D_K = D_MODEL // N_HEADS
        HPG = N_HEADS // N_GROUPS
        EPS = 1e-06

        def rms_norm(x, w):
            rms = jnp.sqrt(jnp.mean(x * x, axis=-1, keepdims=True) + EPS)
            return x / rms * w

        def rope(x):
            d = x.shape[-1]
            half = d // 2
            theta = 1.0 / 10000.0 ** (jnp.arange(half, dtype=jnp.float32) / half)
            pos = jnp.arange(x.shape[1], dtype=jnp.float32)[:, None]
            ang = pos * theta[None, :]
            cos, sin = (jnp.cos(ang), jnp.sin(ang))
            xe, xo = (x[..., 0::2], x[..., 1::2])
            return jnp.concatenate([xe * cos - xo * sin, xe * sin + xo * cos], axis=-1)

        def attention(x, Wq, Wk, Wv, Wo):
            B, S, _ = x.shape
            xr = rope(x)
            Q = (xr @ Wq).reshape(B, S, N_HEADS, D_K).transpose(0, 2, 1, 3)
            Q = Q.reshape(B, N_GROUPS, HPG, S, D_K)
            K = (xr @ Wk).reshape(B, S, N_GROUPS, D_K).transpose(0, 2, 1, 3)
            V = (xr @ Wv).reshape(B, S, N_GROUPS, D_K).transpose(0, 2, 1, 3)
            scores = jnp.einsum('bghsd,bgtd->bghst', Q, K) / jnp.sqrt(jnp.float32(D_K))
            mask = jnp.triu(jnp.full((S, S), -1000000000.0, dtype=scores.dtype), k=1)
            attn = jax.nn.softmax(scores + mask, axis=-1)
            out = jnp.einsum('bghst,bgtd->bghsd', attn, V)
            out = out.reshape(B, N_HEADS, S, D_K).transpose(0, 2, 1, 3).reshape(B, S, D_MODEL)
            return out @ Wo

        def moe(x, router_w, router_b, W1, b1, W2, b2, W3, b3):
            B, S, _ = x.shape
            logits = x @ router_w + router_b
            topv, topi = jax.lax.top_k(logits, TOP_K)
            topw = jax.nn.softmax(topv, axis=-1)
            onehot = jax.nn.one_hot(topi, N_EXPERTS, dtype=x.dtype)
            comb = jnp.einsum('bsk,bske->bse', topw, onehot)
            h1 = jnp.einsum('bsd,edf->ebsf', x, W1) + b1[:, None, None, :]
            h2 = jnp.einsum('bsd,edf->ebsf', x, W2) + b2[:, None, None, :]
            h = h2 * jax.nn.silu(h1)
            eo = jnp.einsum('ebsf,efd->ebsd', h, W3) + b3[:, None, None, :]
            return jnp.einsum('bse,ebsd->bsd', comb, eo)
        h = x + attention(rms_norm(x, norm1_w), Wq, Wk, Wv, Wo)
        h = h + moe(rms_norm(h, norm2_w), router_w, router_b, W1, b1, W2, b2, W3, b3)
        return h
    x = x + _L0_xattn_ref(ctx_1024, _layernorm(x, axis=-1))
    x = x + _L0_ffn_ref(_layernorm(x, axis=-1), L0_ffn_norm1_w, L0_ffn_Wq, L0_ffn_Wk, L0_ffn_Wv, L0_ffn_Wo, L0_ffn_norm2_w, L0_ffn_router_w, L0_ffn_router_b, L0_ffn_W1, L0_ffn_b1, L0_ffn_W2, L0_ffn_b2, L0_ffn_W3, L0_ffn_b3)
    return x

_drawn_inputs = setup_inputs


def setup_inputs(seed=0):
    import zlib

    import numpy as np

    out = dict(_drawn_inputs(seed))
    spreads = {'L0_ffn_norm1_w': (1.0, 0.6),
     'L0_ffn_norm2_w': (1.0, 0.6),
     'L0_ffn_router_b': (0.0, 0.561),
     'L0_ffn_b1': (0.0, 0.8),
     'L0_ffn_b2': (0.0, 0.8),
     'L0_ffn_b3': (0.0, 0.8)}
    factors = {'L0_ffn_Wq': 8.0,
     'L0_ffn_Wk': 8.0,
     'L0_ffn_Wv': 3.483,
     'L0_ffn_Wo': 3.245,
     'L0_ffn_W1': 4.556,
     'L0_ffn_W2': 4.505,
     'L0_ffn_W3': 4.323}
    for name, (base, spread) in spreads.items():
        noise = np.random.default_rng([zlib.crc32(name.encode()), seed]).standard_normal(out[name].shape)
        drawn = base * np.exp(spread * noise) if base else spread * noise
        out[name] = jnp.asarray(drawn.astype(out[name].dtype))
    for name, factor in factors.items():
        out[name] = (out[name] * factor).astype(out[name].dtype)
    return out
```

```python
import concourse.bass as bass
from concourse import mybir
from contextlib import ExitStack

B, S, D = 8, 256, 256
T1 = 120
P = 128
NT = B * S // P
CW, NC = 32, 8
LANES = 16
SLOTS = T1 + NC
SB = 16
PADR = NC - 1
RROWS = PADR + SLOTS
BIG = 1e30
NH, NG, DK = 16, 4, 16
HPG = NH // NG
NE, F = 8, 1024
FC = F // P
GT = 256
CAP = B * S + GT
META = 4
RW = D + META


def xattn_moe_kernel(nc, A, out):
    fp32 = mybir.dt.float32
    f32r = mybir.dt.float32r
    u8 = mybir.dt.uint8
    i32 = mybir.dt.int32
    ALU = mybir.AluOpType
    ACT = mybir.ActivationFunctionType
    AX = mybir.AxisListType.X

    ctx = ExitStack()
    with ctx:
        def sb(name, shape, dt=fp32):
            return ctx.enter_context(nc.sbuf_tensor(name, shape, dt))

        def pb(name, shape, dt=fp32):
            return ctx.enter_context(nc.psum_tensor(name, shape, dt))

        def sem(name):
            return ctx.enter_context(nc.semaphore(name))

        kind = "Internal"
        dsk = nc.dram_tensor("dist_skewed", [SLOTS, P, CW], fp32, kind=kind).ap()
        rcost = nc.dram_tensor("cum_cost", [B, RROWS, S], fp32, kind=kind).ap()
        fptr = nc.dram_tensor("back_ptr", [B, T1, S], u8, kind=kind).ap()

        xs_rows = nc.dram_tensor("expert_rows", [NE * CAP, RW], fp32, kind=kind).ap()

        align_memory = ExitStack()
        arena = align_memory.enter_context(nc.sbuf_tensor("align", [P, 30912], fp32))
        at = [0]

        def carve(rows, *shape, dt=fp32):
            n = 1
            for x in shape:
                n *= x
            if dt == u8:
                n //= 4
            v = arena[0:rows, at[0]:at[0] + n]
            at[0] += n
            if dt != fp32:
                v = v.bitcast(dt)
            if len(shape) == 3:
                return v.rearrange("p (a b c) -> p a b c", a=shape[0], b=shape[1])
            if len(shape) == 2:
                return v.rearrange("p (a b) -> p a b", a=shape[0])
            return v

        DS = carve(P, SLOTS, CW)
        SS = carve(P, SLOTS + 1, CW + 1)
        RA = carve(T1, B, S + 1)
        RB = carve(T1, B, S + 1)
        bigt = arena[:, at[0]:at[0] + 1024]
        FT = carve(B, T1, S, dt=u8)
        C = carve(T1, B, D)
        FV = carve(T1, B, S)
        HV = carve(T1, B, S)
        A0 = carve(T1, B, S)
        A2 = carve(T1, B, S)
        F8 = carve(T1, B, S, dt=u8)
        end_align = at[0]
        at[0] = end_align - 512 - 4 * B * S
        LN = carve(P, 2, 2, D)
        lnT = carve(P, 2, 2 * S)
        sqT = carve(P, 2, 2 * S)
        cT2 = carve(P, 2, 2 * T1)
        dd = carve(T1, B, S)
        csq = carve(T1, D)
        Pm = DS[0:T1, 0:B * S // CW, :].rearrange("p t k -> p (t k)").rearrange("p (b j) -> p b j", b=B)
        align_memory.close()

        WN = 4 * F + FC * D
        wsplit = [sb("wsplit0", [P, 2, WN], f32r)]
        attention_memory = ExitStack()
        arena = attention_memory.enter_context(nc.sbuf_tensor("attention", [P, 2 * WN], fp32))
        at = [0]
        NR = 4
        Sm = carve(P, NR, 3 * P)
        Pe = carve(P, NR, 3 * P)
        PTs = carve(P, NR, 3 * P)
        Z = carve(P, 3, 2, D)
        XN = carve(P, 2, D)
        XR = carve(P, 2, D)
        V = carve(P, 2, 2, NG * DK)
        Oa = carve(P, 2, D)
        OaT = carve(P, 2, S)
        hT = carve(P, 2, S)
        ROW = carve(P, 2, 2, RW)
        attention_memory.close()
        wsplit.append(sb("wsplit1", [P, 2, WN], f32r))
        raw = sb("raw", [P, 2, WN // 3])
        b3b = sb("b3b", [P, NE, D])
        ajunk = sb("ajunk", [P, D])
        assert 4 * WN + 2 * (WN // 3) + NE * D + D >= 30912

        def part(e, k):
            w = wsplit[e % 2]
            return (w[:, k, 0:2 * F].rearrange("p (c n) -> p c n", c=2),
                    w[:, k, 2 * F:4 * F].rearrange("p (c n) -> p c n", c=2),
                    w[:, k, 4 * F:WN].rearrange("p (c n) -> p c n", c=FC))

        X = sb("X", [P, NT, D])
        ident = sb("ident", [P, P])
        identr = sb("identr", [P, P], f32r)
        ones = sb("ones", [P, P])
        tri = sb("tri", [P, P])
        mask = sb("mask", [P, 3 * P])
        iota0 = sb("iota0", [P, S])
        iotah = sb("iotah", [P, S])
        eps5 = sb("eps5", [P, 1])
        eps6 = sb("eps6", [P, 1])
        st = sb("st", [P, NT, 6])
        mv = sb("mv", [P, NT, 2])
        sd = sb("sd", [P, NT])
        rs = sb("rs", [P, NT])
        ms = sb("ms", [P, NT])
        r2 = sb("r2", [P, NT])
        aa = sb("aa", [T1, B])
        mn = sb("mn", [P, CW])
        E = sb("E", [B, T1])
        junk = sb("junk", [P, S])
        EI = sb("EI", [T1, B])
        HI = sb("HI", [T1, B])
        Pt = sb("Pt", [T1, 2, S])

        wqkv = sb("wqkv", [P, 2, D + 2 * NG * DK])
        wo = sb("wo", [P, 2, D])
        wr = sb("wr", [P, 2, NE])
        rbias = sb("rbias", [P, NE])
        n1w = sb("n1w", [P, D])
        n2w = sb("n2w", [P, D])
        cos = sb("cos", [P, 2, D // 2])
        sin = sb("sin", [P, 2, D // 2])
        rt = sb("rt", [P, 2, D // 2])
        xrT = sb("xrT", [P, 2, S])
        QS = sb("QS", [P, 2, NH, 4, DK], f32r)
        KS = sb("KS", [P, 2, NG, 2, 4, DK], f32r)
        QT = sb("QT", [P, 2, NH // 2, S], f32r)
        KT = sb("KT", [P, 2, NG, S], f32r)
        nm = sb("nm", [P, 2, NH, 2])
        rsum = sb("rsum", [P, 2, NH, 2])
        rinv = sb("rinv", [P, NH, 2])
        ssq = sb("ssq", [P, 2])
        lnq = sb("lnq", [P, 2])
        r3 = sb("r3", [P, 2])
        lg = sb("lg", [P, 2, NE])
        lg2 = sb("lg2", [P, 2, NE])
        eq = sb("eq", [P, 2, NE])
        oh1 = sb("oh1", [P, 2, NE])
        oh2 = sb("oh2", [P, 2, NE])
        oh = sb("oh", [P, 2, NE])
        m12 = sb("m12", [P, 2, 2])
        wm = sb("wm", [P, 2])
        ed = sb("ed", [P, 2])
        dn = sb("dn", [P, 2])
        down8 = sb("down8", [P, NE])
        cntE = sb("cntE", [P, NE])
        ecap = sb("ecap", [P, NE])
        idf = sb("idf", [P, NT])
        pose = sb("pose", [P, 2, NE])
        posf = sb("posf", [P, 2, 2])
        pos = sb("pos", [P, 2, 2, 2], i32)
        padrow = sb("padrow", [P, 2, RW])
        fcum = sb("fcum", [1, NE])
        icnt = sb("icnt", [1, NE], i32)
        regs = sb("regs", [1, 2 * NE], i32)
        b1T = sb("b1T", [P, NE, FC])
        b2T = sb("b2T", [P, NE, FC])
        free = X[:, :, :].rearrange("p t d -> p (t d)")
        XS = free[:, 0:2 * RW].rearrange("p (u w) -> p u w", u=2)
        xsH, xsL = KT[:, 0, 0:2, :], KT[:, 0, 2:4, :]
        brow = sb("brow", [NE * FC, 2, P])
        silu = X[:, 4:6, :]
        htmp = X[:, 6:8, :]
        Yt = X[:, 8:10, :]
        Yb = X[:, 10:12, :]
        hH, hL = QT[:, 0], QT[:, 1]
        MT = sb("MT", [P, 2, META])
        MN = sb("MN", [P, 2, META])
        wrow = sb("wrow", [P, 2])
        ids = sb("ids", [P, 2], i32)

        bank = [pb(f"bank{i}", [P, 2, S]) for i in range(8)]
        pT, pC, pD = bank[0:2], bank[2:4], bank[4:6]
        M = bank[0:2]
        SC = bank[2:4]
        XB, HB, YB = bank[0], bank[1:4], bank[4:6]
        PTp = bank[4:6]
        PO = bank[6:8]

        s_x = [sem(f"s_in{b}") for b in range(B)]
        s_cst = sem("s_cst")
        s_pool = sem("s_pool")
        s_corner = sem("s_corner")
        s_fill = sem("s_fill")
        s_v = sem("s_v")
        s_var = sem("s_var")
        s_sd = sem("s_sd")
        s_ln = sem("s_ln")
        s_lnp = sem("s_lnp")
        s_lnT = sem("s_lnT")
        s_cT = sem("s_cT")
        s_aa = sem("s_aa")
        s_d2p = sem("s_d2p")
        s_d2 = sem("s_d2")
        s_dist = sem("s_dist")
        s_dst = sem("s_dst")
        s_dld = [sem(f"s_dld{i}") for i in range(4)]
        s_slot = sem("s_slot")
        s_pre = sem("s_pre")
        s_rst = sem("s_rst")
        s_rld = sem("s_rld")
        s_f8 = sem("s_f8")
        s_fst = sem("s_fst")
        s_fld = sem("s_fld")
        s_e = sem("s_e")
        s_ep = sem("s_ep")
        s_pm = sem("s_pm")
        s_xp = sem("s_xp")
        s_x1 = sem("s_x1")
        s_out = sem("s_out")

        def flat(t):
            return t[:, :, :].rearrange("p b j -> p (b j)")


        s_w = sem("s_w")
        s_b = sem("s_b")
        s_st2 = sem("s_st2")
        s_sq2 = sem("s_sq2")
        s_a = sem("s_a")
        s_g = sem("s_g")
        s_xn = sem("s_xn")
        s_xr = sem("s_xr")
        s_mp = sem("s_mp")
        s_mf = [sem("s_mf0"), sem("s_mf1")]
        s_xrT = sem("s_xrT")
        s_qv = sem("s_qv")
        s_split = sem("s_split")
        s_sc = sem("s_sc")
        s_mx = sem("s_mx")
        s_exp = sem("s_exp")
        s_ptp = sem("s_ptp")
        s_pte = [sem("s_pte0"), sem("s_pte1")]
        s_pv = sem("s_pv")
        s_oa = sem("s_oa")
        s_oaT = sem("s_oaT")
        s_r3 = sem("s_r3")
        s_hn = sem("s_hn")
        s_hT = sem("s_hT")
        s_lg = sem("s_lg")
        s_ed = sem("s_ed")
        s_oh = sem("s_oh")
        s_pos = sem("s_pos")
        s_base = sem("s_base")
        s_bout = sem("s_bout")
        s_sct = [sem("s_sct0"), sem("s_sct1")]
        s_cnt = sem("s_cnt")
        s_padrow = sem("s_padrow")
        s_pad = sem("s_pad")
        s_regs = sem("s_regs")
        s_bT = sem("s_bT")
        s_bTs = sem("s_bTs")
        s_xs = sem("s_xs")
        s_xsp = sem("s_xsp")
        s_xsT = sem("s_xsT")
        s_mt = sem("s_mt")
        s_mm = sem("s_mm")
        s_hp = sem("s_hp")
        s_silu = sem("s_silu")
        s_hb = sem("s_hb")
        s_it = sem("s_it")
        s_raw = [sem("s_raw0"), sem("s_raw1")]
        s_cv = sem("s_cv")
        s_wsp = sem("s_wsp")
        s_hi = sem("s_hi")
        s_hl = sem("s_hl")
        s_xh = sem("s_xh")
        s_yf = sem("s_yf")
        s_y = sem("s_y")
        s_wr = sem("s_wr")
        s_add = sem("s_add")
        s_added = sem("s_added")

        PREP = ["xt", "qkv0", "qkv1", "qt0", "qt1", "kt0", "qt2", "qt3", "kt1"]
        POST = ["ot", "y", "ht", "lg", "rk"]
        AT_PREP = {2: "xt", 3: "qkv0", 4: "qkv1", 6: "qt0", 8: "qt1", 9: "kt0", 11: "qt2", 13: "qt3", 14: "kt1"}
        AT_POST = {5: "ot", 7: "y", 10: "ht", 12: "lg", 15: "rk"}
        LATE_PREP = {4: "qkv0", 5: "qkv1"}
        LATE_POST = {9: "hn", 14: "weights"}
        number = {}
        for name in PREP:
            number[name, 0] = len(number)
        for b in range(B + 1):
            for h in range(NH):
                if h in AT_PREP and b + 1 < B:
                    number[AT_PREP[h], b + 1] = len(number)
                if h in AT_POST and b >= 1:
                    number[AT_POST[h], b - 1] = len(number)

        def read_out(engine, name, b):
            k = number[name, b]
            engine.wait_ge(s_mf[k % 2], k // 2 + 1)

        SHIFT = -4.0 * 1e9
        block = ctx.enter_context(nc.Block())
        NSB = SLOTS // SB

        @block.sync
        def _(sp):
            for b in range(B):
                sp.dma_start(X[:, 2 * b:2 * b + 2, :],
                             A["x"][b].rearrange("(u p) d -> p u d", p=P)).then_inc(s_x[b], 16)
                sp.dma_start(C[:, b, :], A["ctx_1024"][b]).then_inc(s_x[b], 16)
            for u in range(2):
                for t, w in ((cos, "cos"), (sin, "sin")):
                    sp.dma_start(t[:, u, :], A[w][u * P:(u + 1) * P, :]).then_inc(s_w, 16)
            for t, w, o, n in ((wqkv, "Wq", 0, D), (wqkv, "Wk", D, NG * DK), (wqkv, "Wv", D + NG * DK, NG * DK),
                               (wo, "Wo", 0, D), (wr, "router_w", 0, NE)):
                sp.dma_start(t[:, :, o:o + n], A[w].rearrange("(c p) n -> p c n", p=P)).then_inc(s_w, 16)
            for t, w in ((n1w, "norm1_w"), (n2w, "norm2_w"), (rbias, "router_b")):
                sp.dma_start(t[:, :], A[w].partition_broadcast(P)).then_inc(s_w, 16)
            for i, w in enumerate(("b1", "b2")):
                sp.dma_start(brow[:, i, :], A[w].rearrange("e (f p) -> (e f) p", p=P)).then_inc(s_b, 16)
            sp.wait_ge(s_cst, 1)
            for i in range(4):
                sp.dma_start(dsk.rearrange("t p k -> t (p k)")[:, i * 1024:(i + 1) * 1024], bigt[:, :]).then_inc(s_fill, 16)
            sp.dma_start(rcost[:, PADR - 1, 0:CW], bigt[0:B, 0:CW]).then_inc(s_fill, 16)
            sp.wait_ge(s_fill, 80)
            sp.wait_ge(s_dist, 1)
            for b in range(B):
                dst = bass.AP(dsk.tensor, b * LANES * CW + (NC - 1) * CW,
                              [[P * CW, T1], [(P - 1) * CW, NC], [1, CW]])
                sp.dma_start(dst, dd[:, b, :].rearrange("i (c k) -> i c k", c=NC)).then_inc(s_dst, 16)
            sp.wait_ge(s_dst, 128)
            for i in range(4):
                n = SLOTS // 4
                sp.dma_start(DS[:, i * n:(i + 1) * n, :],
                             dsk[i * n:(i + 1) * n].rearrange("t p k -> p t k")).then_inc(s_dld[i], 16)
            for k in range(NSB):
                sp.wait_ge(s_slot, SB * (k + 1))
                for b in range(0, B, 2):
                    dst = bass.AP(rcost.tensor, b * RROWS * S + k * SB * S + (NC - 1) * CW,
                                  [[S - CW, NC], [S, SB], [1, CW]])
                    sp.dma_start(dst, SS[LANES * b:LANES * b + NC, 1 + SB * k:1 + SB * (k + 1), 1:CW + 1]).then_inc(s_rst, 16)
            sp.wait_ge(s_rst, 16 * NSB * B)
            for t, r0 in ((RA, PADR - 1), (RB, PADR)):
                sp.dma_start(t[:, :, 1:S + 1], rcost[:, r0:r0 + T1, :].rearrange("b i j -> i b j")).then_inc(s_rld, 16)
            sp.wait_ge(s_f8, 1)
            sp.dma_start(fptr.rearrange("b i j -> i b j"), F8[:, :, :]).then_inc(s_fst, 16)
            sp.wait_ge(s_fst, 16)
            sp.dma_start(FT[:, :, :], fptr).then_inc(s_fld, 16)
            sp.wait_ge(s_padrow, 3)
            sp.dma_start(out[B * S:B * S + GT, :].rearrange("(u p) d -> p u d", p=P), padrow[:, :, 0:D]).then_inc(s_bout, 16)
            for b in range(B):
                sp.wait_ge(s_base, b + 1)
                sp.dma_start(out[b * S:(b + 1) * S, :].rearrange("(u p) d -> p u d", p=P),
                             X[:, 2 * b:2 * b + 2, :]).then_inc(s_bout, 16)
            sp.wait_ge(s_regs, 1)
            cum = [0] + [sp.value_load(regs[0:1, NE + e:NE + e + 1], min_val=e + 1, max_val=8 * (e + 1)) for e in range(NE)]
            for e in range(NE):
                n = sp.value_load(regs[0:1, e:e + 1], min_val=0, max_val=B * S)
                sp.dma_start(xs_rows[bass.ds(n + e * CAP, GT), :].rearrange("(u p) w -> p u w", p=P),
                             padrow[:, :, :]).then_inc(s_pad, 16)
            sp.wait_ge(s_pad, 16 * NE)
            for q in range(2):
                sp.wait_ge(s_sct[q], 64 * B // 2)
            for e in range(NE):
                with sp.Fori(cum[e], cum[e + 1]) as i:
                    sp.wait_ge(s_xsT, i + 1)
                    sp.wait_ge(s_mt, i + 1)
                    row = nc.s_assert_within((i - cum[e]) * GT + e * CAP, e * CAP, e * CAP + B * S,
                                             skip_runtime_bounds_check_because="a list has B * S rows at most")
                    sp.dma_start(XS, xs_rows[bass.ds(row, GT), :].rearrange("(u p) w -> p u w", p=P)).then_inc(s_xs, 16)
            sp.wait_ge(s_xsT, cum[NE] + 1)
            sp.wait_ge(s_mt, cum[NE] + 1)
            sp.dma_start(XS, xs_rows[0:GT, :].rearrange("(u p) w -> p u w", p=P)).then_inc(s_xs, 16)

        @block.gpsimd
        def _(pool):
            pool.memset(bigt[:, :], BIG).then_inc(s_cst, 1)
            pool.memset(ident[:, :], 0.0).then_inc(s_pool, 1)
            pool.memset(ones[:, :], 1.0)
            pool.memset(eps5[:, :], 1e-5)
            pool.iota(iota0[:, :], pattern=[[1, S]], base=0, channel_multiplier=0,
                      allow_small_or_imprecise_dtypes=True)
            pool.iota(iotah[:, :], pattern=[[2, S]], base=1, channel_multiplier=0,
                      allow_small_or_imprecise_dtypes=True)
            pool.wait_ge(s_pool, 1)
            pool.affine_select(out=ident[:, :], in_=ident[:, :], compare_op=ALU.not_equal, fill=1.0,
                               base=0, pattern=[[-1, P]], channel_multiplier=1).then_inc(s_cst, 1)
            pool.memset(SS[:, 0, :], BIG).then_inc(s_pool, 1)
            pool.memset(RA[:, :, 0:1], BIG).then_inc(s_pool, 1)
            pool.memset(RB[:, :, 0:1], BIG).then_inc(s_pool, 1)
            pool.wait_ge(s_pool, 2)
            pool.dma_start(SS[:, 0, 0:1], A["corner"]).then_inc(s_corner, 16)

            pool.memset(tri[:, :], 1.0).then_inc(s_pool, 1)
            pool.memset(mask[:, :], 0.0).then_inc(s_pool, 1)
            pool.memset(eps6[:, :], 1e-6)
            pool.iota(idf[:, :], pattern=[[P, NT]], base=0, channel_multiplier=1, allow_small_or_imprecise_dtypes=True)
            pool.iota(down8[:, :], pattern=[[-1, NE]], base=NE, channel_multiplier=0, allow_small_or_imprecise_dtypes=True)
            pool.iota(ecap[:, :], pattern=[[CAP, NE]], base=0, channel_multiplier=0, allow_small_or_imprecise_dtypes=True)
            pool.iota(cntE[:, :], pattern=[[CAP, NE]], base=0, channel_multiplier=0, allow_small_or_imprecise_dtypes=True)
            pool.memset(padrow[:, :, :], 0.0).then_inc(s_padrow, 1)
            pool.wait_ge(s_padrow, 1)
            for u in range(2):
                pool.iota(padrow[:, u, D:D + 1], pattern=[[0, 1]], base=B * S + u * P, channel_multiplier=1,
                          allow_small_or_imprecise_dtypes=True).then_inc(s_padrow, 1)
            pool.wait_ge(s_pool, 6)
            pool.affine_select(out=tri[:, :], in_=tri[:, :], compare_op=ALU.is_gt, fill=0.0, base=0,
                               pattern=[[1, P]], channel_multiplier=-1).then_inc(s_cst, 1)
            for o in (0, 2 * P):
                pool.affine_select(out=mask[:, o:o + P], in_=mask[:, o:o + P], compare_op=ALU.is_ge, fill=SHIFT, base=0,
                                   pattern=[[-1, P]], channel_multiplier=1).then_inc(s_cst, 1)
            g = [0]

            def link(ins):
                g[0] += 1
                ins.then_inc(s_g, 1)
                pool.wait_ge(s_g, g[0])

            def rope(b):
                pool.wait_ge(s_xn, b + 1)
                if b:
                    pool.wait_ge(s_mp, number["xt", b - 1] + 1)
                x2 = XN[:, :, :].rearrange("p u (i two) -> p u i two", two=2)
                xe, xo = x2[:, :, :, 0], x2[:, :, :, 1]
                hd = D // 2
                pool.tensor_tensor(XR[:, :, 0:hd], xe, cos[:, :, :], ALU.mult)
                link(pool.tensor_tensor(rt[:, :, :], xo, sin[:, :, :], ALU.mult))
                link(pool.tensor_tensor(XR[:, :, 0:hd], XR[:, :, 0:hd], rt[:, :, :], ALU.subtract))
                pool.tensor_tensor(XR[:, :, hd:D], xe, sin[:, :, :], ALU.mult)
                link(pool.tensor_tensor(rt[:, :, :], xo, cos[:, :, :], ALU.mult))
                pool.tensor_tensor(XR[:, :, hd:D], XR[:, :, hd:D], rt[:, :, :], ALU.add).then_inc(s_xr, 1)

            def rows_out(c):
                q = c % 2
                pool.wait_ge(s_pos, c + 1)
                for u in range(2):
                    for k in range(2):
                        pool.indirect_dma_start(xs_rows, bass.IndirectOffsetOnAxis(pos[:, q, u, k:k + 1], 0),
                                                ROW[:, q, u, :], None).then_inc(s_sct[q], 16)

            def fetch(n):
                w = A[("W1", "W2", "W3")[n % 3]][n // 3].rearrange("(c p) n -> p c n", p=P)
                c = 2 if n % 3 < 2 else FC
                pool.dma_start(raw[:, n % 2, :].rearrange("p (c n) -> p c n", c=c), w).then_inc(s_raw[n % 2], 16)

            def convert(e):
                for n in range(3 * e, 3 * e + 3):
                    o = slice(n % 3 * (WN // 3), (n % 3 + 1) * (WN // 3))
                    hi, lo = wsplit[e % 2][:, 0, o], wsplit[e % 2][:, 1, o]
                    pool.wait_ge(s_raw[n % 2], 16 * (n // 2 + 1))
                    pool.tensor_scalar(hi, raw[:, n % 2, :], 1.0, 1.0, ALU.mult, ALU.mult).then_inc(s_cv, 1)
                    pool.wait_ge(s_cv, 2 * n + 1)
                    pool.tensor_tensor(lo, raw[:, n % 2, :], hi.bitcast(fp32), ALU.subtract).then_inc(s_cv, 1)
                    if n + 2 < 3 * NE:
                        pool.wait_ge(s_cv, 2 * n + 2)
                        fetch(n + 2)

            pool.wait_ge(s_w, 16 * 12)
            pool.wait_ge(s_x1, 2 * B)
            fetch(0)
            fetch(1)
            rope(0)
            for b in range(B + 1):
                if b + 1 < B:
                    rope(b + 1)
                if b == 0:
                    convert(0)
                if b >= 2:
                    rows_out(b - 2)
                if b >= 1:
                    c, z = b - 1, (b - 1) % 3
                    read_out(pool, "y", c)
                    pool.tensor_tensor(X[:, 2 * c:2 * c + 2, :], X[:, 2 * c:2 * c + 2, :], Z[:, z, :, :], ALU.add).then_inc(s_base, 1)
            rows_out(B - 1)
            pool.wait_ge(s_bout, 16 * (B + 1))
            pool.wait_ge(s_regs, 1)
            for q in range(2):
                pool.wait_ge(s_sct[q], 64 * B // 2)
            cum = [0] + [pool.value_load(regs[0:1, NE + e:NE + e + 1], min_val=e + 1, max_val=8 * (e + 1)) for e in range(NE)]
            for e in range(NE):
                if e + 1 < NE:
                    if e:
                        pool.wait_ge(s_it, cum[e])
                        pool.sem_inc(s_padrow, 1)
                    convert(e + 1)
                with pool.Fori(cum[e], cum[e + 1]) as i:
                    pool.wait_ge(s_y, i + 1)
                    pool.sem_inc(s_padrow, 1)
                    for u in range(2):
                        pool.indirect_dma_start(out, bass.IndirectOffsetOnAxis(ids[:, u:u + 1], 0),
                                                Yb[:, u, :], None, compute_op=ALU.add).then_inc(s_add, 16)
                    pool.wait_ge(s_add, 32 * i + 32)
                    pool.sem_inc(s_added, 1)


        @block.scalar
        def _(act):
            act.wait_ge(s_cst, 2)
            act.wait_ge(s_var, 1)
            act.activation(sd[:, :], mv[:, :, 1], ACT.Sqrt, bias=eps5[:, :]).then_inc(s_sd, 1)
            for b in range(B):
                q = b % 2
                act.wait_ge(s_x[b], 32)
                if b:
                    act.wait_ge(s_aa, b)
                act.activation(csq[:, :], C[:, b, :], ACT.Square, accum_out=aa[:, b:b + 1]).then_inc(s_aa, 1)
                act.wait_ge(s_lnp, b + 1)
                if b >= 2:
                    act.wait_ge(s_d2p, b - 1)
                act.activation(lnT[:, q], flat(pT[q]), ACT.Copy)
                act.activation(sqT[:, q], flat(pT[q]), ACT.Square).then_inc(s_lnT, 1)
            act.wait_ge(s_d2, B)
            act.activation(dd[:, :, :], dd[:, :, :], ACT.Sqrt).then_inc(s_dist, 1)
            for k in range(NSB):
                act.wait_ge(s_slot, SB * (k + 1))
                for b in range(1, B, 2):
                    dst = bass.AP(rcost.tensor, b * RROWS * S + k * SB * S + (NC - 1) * CW,
                                  [[S - CW, NC], [S, SB], [1, CW]])
                    act.dma_start(dst, SS[LANES * b:LANES * b + NC, 1 + SB * k:1 + SB * (k + 1), 1:CW + 1]).then_inc(s_rst, 16)
            n = [0]

            def link(ins):
                n[0] += 1
                ins.then_inc(s_a, 1)
                act.wait_ge(s_a, n[0])

            act.wait_ge(s_st2, 1)
            act.activation(sd[:, :], mv[:, :, 1], ACT.Sqrt, bias=eps5[:, :]).then_inc(s_sq2, 1)
            act.wait_ge(s_padrow, 3)
            act.wait_ge(s_st2, 2)
            act.activation(sd[:, :], ms[:, :], ACT.Sqrt, bias=eps6[:, :]).then_inc(s_sq2, 1)
            act.wait_ge(s_w, 16 * 12)
            act.wait_ge(s_x1, 2 * B)
            act.dma_start(b3b[:, :, :], A["b3"].partition_broadcast(P)).then_inc(s_b, 16)

            def filled(name, b):
                k = number[name, b]
                act.wait_ge(s_mp, k + 1)
                return M[k % 2], s_mf[k % 2]

            def prep(name, b):
                q = b % 2
                if name == "xt":
                    m, free = filled(name, b)
                    if b:
                        act.wait_ge(s_mp, number["qkv1", b - 1] + 1)
                    act.activation(xrT[:, :, :], m[:, :, :], ACT.Copy).then_inc(free, 1)
                elif name in ("qkv0", "qkv1"):
                    u = int(name[3])
                    m, free = filled(name, b)
                    pq = flat(m)
                    if b >= 2:
                        act.wait_ge(s_pv, NH * (b - 1))
                    if b and u == 0:
                        act.wait_ge(s_mp, number["kt1", b - 1] + 1)
                    act.activation(V[:, q, u, :], pq[:, D + NG * DK:D + 2 * NG * DK], ACT.Copy)
                    act.activation(QS[:, u, :, 0:4:2, :],
                                   pq[:, 0:D].rearrange("p (h d) -> p h d", h=NH).unsqueeze(2).to_broadcast([P, NH, 2, DK]),
                                   ACT.Copy)
                    act.activation(KS[:, u, :, 0, 0:2, :],
                                   pq[:, D:D + NG * DK].rearrange("p (h d) -> p h d", h=NG).unsqueeze(2).to_broadcast([P, NG, 2, DK]),
                                   ACT.Copy).then_inc(s_qv, 1)
                elif name in ("qt1", "qt3"):
                    m, free = filled(name, b)
                    u = int(name[2]) // 2
                    if b >= 2:
                        act.wait_ge(s_sc, NH * (b - 1))
                    act.activation(QT[:, q, NH // 4:NH // 2, u * P:(u + 1) * P],
                                   flat(m).rearrange("p (a s) -> p a s", a=4), ACT.Copy).then_inc(free, 1)

            def post(name, b):
                q, z = b % 2, b % 3
                if name == "ot":
                    m, free = filled(name, b)
                    act.activation(OaT[:, :, :], m[:, :, :], ACT.Copy).then_inc(free, 1)
                elif name == "r3":
                    read_out(act, "y", b)
                    for u in range(2):
                        link(act.activation(ajunk[:, :], Z[:, z, u, :], ACT.Square, accum_out=ssq[:, u:u + 1]))
                    link(act.activation(lnq[:, :], ssq[:, :], ACT.Ln, bias=eps6[:, :], scale=1.0 / D))
                    act.activation(r3[:, :], lnq[:, :], ACT.Exp, scale=-0.5).then_inc(s_r3, 1)
                elif name == "ht":
                    m, free = filled(name, b)
                    act.activation(hT[:, :, :], m[:, :, :], ACT.Copy).then_inc(free, 1)
                elif name == "lg":
                    act.wait_ge(s_lg, b + 1)
                    act.activation(ed[:, :], ed[:, :], ACT.Exp).then_inc(s_ed, 1)

            def exps(g):
                q, h = (g // NH) % 2, g % NH
                act.wait_ge(s_mx, g + 1)
                if g >= NR:
                    act.wait_ge(s_ptp, g - NR + 1)
                r = g % NR
                act.activation(Pe[:, r, 0:P], Sm[:, r, 0:P], ACT.Exp, bias=nm[:, q, h, 0:1], scale=-1.0,
                               accum_out=rsum[:, q, h, 0:1])
                act.activation(Pe[:, r, P:3 * P], Sm[:, r, P:3 * P], ACT.Exp, bias=nm[:, q, h, 1:2], scale=-1.0,
                               accum_out=rsum[:, q, h, 1:2]).then_inc(s_exp, 1)

            def evac(g):
                act.wait_ge(s_ptp, g + 1)
                if g >= NR:
                    act.wait_ge(s_pv, g - NR + 1)
                act.activation(PTs[:, g % NR, :], flat(PTp[g % 2])[:, 0:3 * P], ACT.Copy).then_inc(s_pte[g % 2], 1)

            for name in PREP:
                prep(name, 0)
            for b in range(B + 1):
                for h in range(NH):
                    g = b * NH + h
                    if g % 2 == 1 and 3 <= g < B * NH + 3:
                        evac(g - 3)
                    if h == 8 and b >= 1:
                        post("r3", b - 1)
                    if g < B * NH:
                        exps(g)
                    if h in AT_PREP and b + 1 < B:
                        prep(AT_PREP[h], b + 1)
                    if h in AT_POST and b >= 1:
                        post(AT_POST[h], b - 1)

            act.wait_ge(s_bTs, 1)
            act.wait_ge(s_regs, 1)
            cum = [0] + [act.value_load(regs[0:1, NE + e:NE + e + 1], min_val=e + 1, max_val=8 * (e + 1)) for e in range(NE)]
            act.wait_ge(s_xsp, 1)
            act.activation(xsH, XB[:, :, :], ACT.Copy).then_inc(s_xh, 1)
            for e in range(NE):
                with act.Fori(cum[e], cum[e + 1]) as i:
                    for f in range(FC):
                        act.wait_ge(s_hp, i * FC + f + 1)
                        act.wait_ge(s_hb, i * FC + f + 2)
                        act.activation(silu[:, f % 2, :], HB[f % 3][:, 0, :], ACT.Silu,
                                       bias=b1T[:, e, f:f + 1]).then_inc(s_silu, 1)
                    act.wait_ge(s_xsp, i + 2)
                    act.activation(xsH, XB[:, :, :], ACT.Copy).then_inc(s_xh, 1)

        @block.tensor
        def _(pe):
            pe.wait_ge(s_cst, 2)

            def dist(b):
                q = b % 2
                pe.wait_ge(s_lnT, b + 1)
                pe.wait_ge(s_cT, b + 1)
                if b >= 2:
                    pe.wait_ge(s_d2, b - 1)
                o = pD[q][0:T1, 0, :]
                for c in range(2):
                    pe.matmul(o, cT2[:, q, c * T1:(c + 1) * T1], lnT[:, q, c * S:(c + 1) * S], start=(c == 0), stop=False)
                    last = pe.matmul(o, ones[:, 0:T1], sqT[:, q, c * S:(c + 1) * S], start=False, stop=(c == 1))
                last.then_inc(s_d2p, 1)

            for b in range(B):
                q = b % 2
                pe.wait_ge(s_ln, 2 * b + 2)
                pe.wait_ge(s_x[b], 32)
                if b >= 2:
                    pe.wait_ge(s_lnT, b - 1)
                    pe.wait_ge(s_cT, b - 1)
                for c in range(2):
                    for u in range(2):
                        pe.transpose(pT[q][:, c, u * P:(u + 1) * P], LN[:, b % 2, u, c * P:(c + 1) * P], ident[:, :])
                for c in range(2):
                    last = pe.transpose(pC[q][:, c, 0:T1], C[:, b, c * P:(c + 1) * P], ident[0:T1, 0:T1])
                last.then_inc(s_lnp, 1)
                if b:
                    dist(b - 1)
            dist(B - 1)
            pe.wait_ge(s_e, 1)
            pe.transpose(pC[0][0:T1, 0, 0:B], E[:, :], ident[0:B, 0:B]).then_inc(s_ep, 1)
            for b in range(B):
                q = b % 2
                pe.wait_ge(s_pm, b + 1)
                if b >= 2:
                    pe.wait_ge(s_x1, 2 * (b - 1))
                for u in range(2):
                    last = pe.matmul(pT[q][:, u, :], Pm[:, b, u * P:(u + 1) * P], C[:, b, :], start=True, stop=True)
                last.then_inc(s_xp, 1)


            pe.wait_ge(s_w, 16 * 12)
            pe.wait_ge(s_cst, 5)
            pe.wait_ge(s_b, 32)
            for i in range(2):
                last = pe.transpose(bank[6][:, i, 0:NE * FC], brow[:, i, :], ident[0:NE * FC, 0:NE * FC])
            last.then_inc(s_bT, 1)

            def slot(name, b):
                k = number[name, b]
                if k < 2:
                    pe.wait_ge(s_x1, 2 * B)
                if k // 2:
                    pe.wait_ge(s_mf[k % 2], k // 2)
                return M[k % 2]

            def prep(name, b):
                q = b % 2
                m = slot(name, b)
                f = flat(m)
                if name == "xt":
                    pe.wait_ge(s_xr, b + 1)
                    for c in range(2):
                        for u in range(2):
                            last = pe.transpose(m[:, c, u * P:(u + 1) * P], XR[:, u, c * P:(c + 1) * P], ident[:, :])
                elif name in ("qkv0", "qkv1"):
                    u = int(name[3])
                    read_out(pe, "xt", b)
                    for c in range(2):
                        last = pe.matmul(f[:, 0:D + 2 * NG * DK], xrT[:, c, u * P:(u + 1) * P], wqkv[:, c, :],
                                         start=(c == 0), stop=(c == 1))
                elif name[0] == "q":
                    i = int(name[2])
                    u, a = i // 2, i % 2
                    pe.wait_ge(s_split, 2 * b + u + 1)
                    for j in range(4):
                        h = 8 * a + 2 * j
                        last = pe.transpose(f[:, j * P:(j + 1) * P].bitcast(f32r),
                                            QS[:, u, h:h + 2, :, :].rearrange("p h a d -> p (h a d)"), identr[:, :])
                else:
                    u = int(name[2])
                    read_out(pe, f"qkv{u}", b)
                    for j in range(NG):
                        last = pe.transpose(f[:, j * P:(j + 1) * P].bitcast(f32r),
                                            KS[:, u, j, :, :, :].rearrange("p h a d -> p (h a d)"), identr[:, :])
                last.then_inc(s_mp, 1)

            def post(name, b):
                q, z = b % 2, b % 3
                m = slot(name, b)
                if name == "ot":
                    pe.wait_ge(s_oa, b + 1)
                    for c in range(2):
                        for u in range(2):
                            last = pe.transpose(m[:, c, u * P:(u + 1) * P], Oa[:, u, c * P:(c + 1) * P], ident[:, :])
                elif name == "y":
                    read_out(pe, "ot", b)
                    for u in range(2):
                        for c in range(2):
                            last = pe.matmul(m[:, u, :], OaT[:, c, u * P:(u + 1) * P], wo[:, c, :],
                                             start=(c == 0), stop=(c == 1))
                elif name == "ht":
                    pe.wait_ge(s_hn, b + 1)
                    for c in range(2):
                        for u in range(2):
                            last = pe.transpose(m[:, c, u * P:(u + 1) * P], ROW[:, q, u, c * P:(c + 1) * P], ident[:, :])
                elif name == "lg":
                    read_out(pe, "ht", b)
                    for u in range(2):
                        for c in range(2):
                            last = pe.matmul(m[:, 0, u * NE:(u + 1) * NE], hT[:, c, u * P:(u + 1) * P], wr[:, c, :],
                                             start=(c == 0), stop=(c == 1))
                else:
                    pe.wait_ge(s_oh, b + 1)
                    pe.matmul(m[:, 0, 0:NE], tri[:, :], oh[:, 0, :], start=True, stop=True)
                    pe.matmul(m[:, 0, NE:2 * NE], tri[:, :], oh[:, 1, :], start=True, stop=False)
                    pe.matmul(m[:, 0, NE:2 * NE], ones[:, :], oh[:, 0, :], start=False, stop=True)
                    pe.matmul(m[:, 0, 2 * NE:3 * NE], ones[:, :], oh[:, 0, :], start=True, stop=False)
                    last = pe.matmul(m[:, 0, 2 * NE:3 * NE], ones[:, :], oh[:, 1, :], start=False, stop=True)
                last.then_inc(s_mp, 1)

            def scores(g):
                b, h = g // NH, g % NH
                q, o, grp = b % 2, 64 * (h % 2), h // HPG
                if h == 0:
                    for name in ("qt0", "qt1", "kt0", "qt2", "qt3", "kt1"):
                        read_out(pe, name, b)
                if g >= 2:
                    pe.wait_ge(s_mx, g - 1)
                f = flat(SC[g % 2])
                for u in range(2):
                    n = P * (u + 1)
                    last = pe.matmul(f[:, u * P:u * P + n], QT[o:o + 64, q, h // 2, u * P:(u + 1) * P],
                                     KT[o:o + 64, q, grp, 0:n], start=True, stop=True)
                last.then_inc(s_sc, 1)

            def turn(g):
                pe.wait_ge(s_exp, g + 1)
                if g >= 2:
                    pe.wait_ge(s_pte[g % 2], g // 2)
                f = flat(PTp[g % 2])
                for j in range(3):
                    last = pe.transpose(f[:, j * P:(j + 1) * P], Pe[:, g % NR, j * P:(j + 1) * P], ident[:, :])
                last.then_inc(s_ptp, 1)

            def pv(g):
                b, h = g // NH, g % NH
                q, grp, r = b % 2, h // HPG, g % NR
                pe.wait_ge(s_pte[g % 2], g // 2 + 1)
                if b >= 2 and h == 0:
                    pe.wait_ge(s_oa, b - 1)
                if g == 0:
                    pe.wait_ge(s_bTs, 1)
                o = slice(h * DK, (h + 1) * DK)
                kv = slice(grp * DK, (grp + 1) * DK)
                pe.matmul(PO[q][:, 0, o], PTs[:, r, 0:P], V[:, q, 0, kv], start=True, stop=True)
                pe.matmul(PO[q][:, 1, o], PTs[:, r, P:2 * P], V[:, q, 0, kv], start=True, stop=False)
                pe.matmul(PO[q][:, 1, o], PTs[:, r, 2 * P:3 * P], V[:, q, 1, kv], start=False, stop=True).then_inc(s_pv, 1)

            for name in PREP:
                prep(name, 0)
            for b in range(B + 1):
                for h in range(NH):
                    g = b * NH + h
                    if g < B * NH:
                        scores(g)
                    if 2 <= g < B * NH + 2:
                        turn(g - 2)
                    if 4 <= g < B * NH + 4:
                        pv(g - 4)
                    if h in AT_PREP and b + 1 < B:
                        prep(AT_PREP[h], b + 1)
                    if h in AT_POST and b >= 1:
                        post(AT_POST[h], b - 1)

            pe.wait_ge(s_regs, 1)
            cum = [0] + [pe.value_load(regs[0:1, NE + e:NE + e + 1], min_val=e + 1, max_val=8 * (e + 1)) for e in range(NE)]

            def turn_rows():
                for c in range(2):
                    for u in range(2):
                        last = pe.transpose(XB[:, c, u * P:(u + 1) * P], XS[:, u, c * P:(c + 1) * P], ident[:, :])
                last.then_inc(s_xsp, 1)

            pe.wait_ge(s_xs, 16)
            turn_rows()
            for e in range(NE):
                q = e % 2
                pe.wait_ge(s_cv, 6 * e + 6)
                (H1, H2, H3), (L1, L2, L3) = part(e, 0), part(e, 1)
                with pe.Fori(cum[e], cum[e + 1]) as i:
                    pe.wait_ge(s_xsT, i + 2)
                    for f in range(FC + 2):
                        if f < FC:
                            pe.wait_ge(s_hb, i * FC + f + 1)
                            o = slice(f * P, (f + 1) * P)
                            for j, (wh, wl) in enumerate(((H1, L1), (H2, L2))):
                                for c in range(2):
                                    for k, (w, x) in enumerate(((wh, xsH), (wh, xsL), (wl, xsH))):
                                        last = pe.matmul(HB[f % 3][:, j, :], w[:, c, o], x[:, c, :],
                                                         start=(c == 0 and k == 0), stop=(c == 1 and k == 2))
                            last.then_inc(s_hp, 1)
                        if f == FC:
                            pe.wait_ge(s_xs, i * 16 + 32)
                            turn_rows()
                        if f >= 2:
                            g = f - 2
                            pe.wait_ge(s_hl, i * FC + g + 1)
                            if g == 0:
                                pe.wait_ge(s_yf, i + 1)
                            for u in range(2):
                                o = slice(u * P, (u + 1) * P)
                                for k, (hh, w) in enumerate(((hH, H3), (hH, L3), (hL, H3))):
                                    last = pe.matmul(YB[u][:, 0, :], hh[:, g, o], w[:, g, :],
                                                     start=(g == 0 and k == 0), stop=(g == FC - 1 and k == 2))
                    last.then_inc(s_it, 1)

        @block.vector
        def _(dve):
            n = [0]

            def link(ins):
                n[0] += 1
                ins.then_inc(s_v, 1)
                dve.wait_ge(s_v, n[0])

            for b in range(B):
                dve.wait_ge(s_x[b], 32)
                for u in (2 * b, 2 * b + 1):
                    last = dve.bn_stats(st[:, u, :], X[:, u, :])
            link(last)
            for u in range(NT):
                last = dve.bn_aggr(mv[:, u, :], st[:, u, :])
            last.then_inc(s_var, 1)
            dve.wait_ge(s_sd, 1)
            link(dve.reciprocal(rs[:, :], sd[:, :]))

            def d2(b):
                q = b % 2
                dve.wait_ge(s_d2p, b + 1)
                dve.wait_ge(s_aa, b + 1)
                dve.tensor_scalar(dd[:, b, :], pD[q][0:T1, 0, :], aa[:, b:b + 1], 0.0, ALU.add, ALU.max).then_inc(s_d2, 1)

            for b in range(B):
                q = b % 2
                if b >= 2:
                    dve.wait_ge(s_lnp, b - 1)
                for u in (2 * b, 2 * b + 1):
                    dve.tensor_scalar(LN[:, b % 2, u % 2, :], X[:, u, :], mv[:, u, 0:1], rs[:, u:u + 1],
                                      ALU.subtract, ALU.mult).then_inc(s_ln, 1)
                dve.wait_ge(s_lnp, b + 1)
                if b >= 2:
                    dve.wait_ge(s_d2p, b - 1)
                dve.tensor_scalar(cT2[:, q].rearrange("p (c i) -> p c i", c=2), pC[q][:, :, 0:T1], -2.0, None, ALU.mult).then_inc(s_cT, 1)
                if b:
                    d2(b - 1)
            d2(B - 1)

            dve.wait_ge(s_corner, 16)
            shift = [i + 1 if i % LANES != LANES - 1 else i for i in range(32)]
            for t in range(SLOTS):
                if t % (SLOTS // 4) == 0:
                    dve.wait_ge(s_dld[t // (SLOTS // 4)], 16)
                if t:
                    dve.wait_ge(s_slot, t)
                dve.tensor_tensor(mn[:, :], SS[:, t, 0:CW], SS[:, t, 1:CW + 1], ALU.min).then_inc(s_pre, 1)
                dve.stream_shuffle(SS[:, t + 1, 0:1], SS[:, t, CW:CW + 1], shift).then_inc(s_pre, 1)
                dve.wait_ge(s_pre, 2 * (t + 1))
                dve.tensor_tensor_scan(SS[:, t + 1, 1:CW + 1], mn[:, :], DS[:, t, :], SS[:, t + 1, 0:1],
                                       ALU.min, ALU.add).then_inc(s_slot, 1)

            dve.wait_ge(s_rld, 32)
            dve.wait_ge(s_pool, 4)
            cd, cu, cl = RA[:, :, 0:S], RA[:, :, 1:S + 1], RB[:, :, 0:S]
            io = iota0[0:T1, :].unsqueeze(1).to_broadcast([T1, B, S])
            ih = iotah[0:T1, :].unsqueeze(1).to_broadcast([T1, B, S])
            link(dve.tensor_tensor(A0[:, :, :], cu, cl, ALU.min))
            link(dve.tensor_tensor(A0[:, :, :], cd, A0[:, :, :], ALU.is_le))
            link(dve.tensor_tensor(A2[:, :, :], cl, cu, ALU.is_lt))
            link(dve.tensor_tensor(A2[:, :, :], A2[:, :, :], A0[:, :, :], ALU.is_gt))
            link(dve.tensor_tensor(FV[:, :, :], io, A0[:, :, :], ALU.subtract))
            link(dve.scalar_tensor_tensor(flat(FV), flat(A2), 0.0, flat(FV), ALU.is_equal, ALU.mult))
            dve.tensor_tensor_scan(flat(F8), flat(A2), flat(FV), 0.0, ALU.mult, ALU.max).then_inc(s_f8, 1)
            link(dve.tensor_tensor(HV[:, :, :], ih, A0[:, :, :], ALU.subtract))
            link(dve.scalar_tensor_tensor(flat(HV), flat(A2), 0.0, flat(HV), ALU.is_equal, ALU.mult))
            link(dve.tensor_tensor_scan(flat(HV), flat(A2), flat(HV), 0.0, ALU.mult, ALU.max))
            link(dve.memset(E[:, T1 - 1:T1], float(S - 1)))
            dve.wait_ge(s_fld, 16)
            for i in range(T1 - 1, 0, -1):
                ins = dve.scalar_tensor_tensor(junk[0:B, :], iota0[0:B, :], E[:, i:i + 1], FT[:, i, :],
                                               ALU.is_equal, ALU.mult, accum_out=E[:, i - 1:i])
                if i > 1:
                    link(ins)
            ins.then_inc(s_e, 1)
            dve.wait_ge(s_ep, 1)
            link(dve.tensor_copy(EI[:, :], pC[0][0:T1, 0, 0:B]))
            for b in range(B):
                link(dve.scalar_tensor_tensor(junk[0:T1, :], iota0[0:T1, :], EI[:, b:b + 1], HV[:, b, :],
                                              ALU.is_equal, ALU.mult, accum_out=HI[:, b:b + 1]))

            def add_x(b):
                dve.wait_ge(s_xp, b + 1)
                for u in range(2):
                    dve.tensor_tensor(X[:, 2 * b + u, :], X[:, 2 * b + u, :], pT[b % 2][:, u, :], ALU.add).then_inc(s_x1, 1)

            for b in range(B):
                link(dve.tensor_scalar(Pt[:, b % 2, :], iotah[0:T1, :], HI[:, b:b + 1], None, ALU.is_ge))
                dve.scalar_tensor_tensor(Pm[:, b, :], iota0[0:T1, :], EI[:, b:b + 1], Pt[:, b % 2, :],
                                         ALU.is_le, ALU.mult).then_inc(s_pm, 1)
                if b:
                    add_x(b - 1)
            add_x(B - 1)
            dve.wait_ge(s_x1, 2 * B)
            for u in range(NT):
                last = dve.bn_stats(st[:, u, :], X[:, u, :])
            link(last)
            for u in range(NT):
                last = dve.bn_aggr(mv[:, u, :], st[:, u, :])
            last.then_inc(s_st2, 1)
            dve.wait_ge(s_sq2, 1)
            link(dve.reciprocal(rs[:, :], sd[:, :]))
            link(dve.tensor_tensor(ms[:, :], mv[:, :, 1], rs[:, :], ALU.mult))
            dve.tensor_tensor(ms[:, :], ms[:, :], rs[:, :], ALU.mult).then_inc(s_st2, 1)
            dve.wait_ge(s_sq2, 2)
            link(dve.reciprocal(r2[:, :], sd[:, :]))
            dve.wait_ge(s_w, 16 * 12)
            dve.wait_ge(s_cst, 5)
            dve.wait_ge(s_padrow, 3)
            link(dve.tensor_copy(identr[:, :], ident[:, :]))
            dve.wait_ge(s_bT, 1)
            dve.tensor_copy(b1T[:, :, :].rearrange("p e f -> p (e f)"), bank[6][:, 0, 0:NE * FC])
            dve.tensor_copy(b2T[:, :, :].rearrange("p e f -> p (e f)"), bank[6][:, 1, 0:NE * FC]).then_inc(s_bTs, 1)

            def norms(b):
                z = b % 3
                if b >= 3:
                    dve.wait_ge(s_base, b - 2)
                for u in range(2):
                    t = 2 * b + u
                    last = dve.tensor_scalar(Z[:, z, u, :], X[:, t, :], mv[:, t, 0:1], rs[:, t:t + 1], ALU.subtract, ALU.mult)
                link(last)
                if b:
                    dve.wait_ge(s_xr, b)
                for u in range(2):
                    t = 2 * b + u
                    last = dve.scalar_tensor_tensor(XN[:, u, :], Z[:, z, u, :], r2[:, t:t + 1], n1w[:, :], ALU.mult, ALU.mult)
                last.then_inc(s_xn, 1)

            def filled(name, b):
                k = number[name, b]
                dve.wait_ge(s_mp, k + 1)
                return M[k % 2], s_mf[k % 2]

            def prep(name, b):
                q = b % 2
                if name in ("qkv0", "qkv1"):
                    u = int(name[3])
                    k = number[name, b]
                    pq = flat(M[k % 2])
                    dve.wait_ge(s_qv, 2 * b + u + 1)
                    dve.tensor_tensor(QS[:, u, :, 1:4:2, :],
                                      pq[:, 0:D].rearrange("p (h d) -> p h d", h=NH).unsqueeze(2).to_broadcast([P, NH, 2, DK]),
                                      QS[:, u, :, 0:4:2, :].bitcast(fp32), ALU.subtract).then_inc(s_split, 1)
                    link(dve.tensor_tensor(KS[:, u, :, 0, 2:4, :],
                                           pq[:, D:D + NG * DK].rearrange("p (h d) -> p h d", h=NG).unsqueeze(2).to_broadcast([P, NG, 2, DK]),
                                           KS[:, u, :, 0, 0:2, :].bitcast(fp32), ALU.subtract))
                    dve.tensor_copy(KS[:, u, :, 1, :, :].rearrange("p g a d -> p g (a d)"),
                                    KS[:, u, :, 0, :, :].rearrange("p g a d -> p g (a d)").bitcast(fp32)).then_inc(s_mf[k % 2], 1)
                elif name in ("qt0", "qt2"):
                    m, free = filled(name, b)
                    u = int(name[2]) // 2
                    if b >= 2:
                        dve.wait_ge(s_sc, NH * (b - 1))
                    dve.tensor_copy(QT[:, q, 0:NH // 4, u * P:(u + 1) * P],
                                    flat(m).rearrange("p (a s) -> p a s", a=4)).then_inc(free, 1)
                elif name in ("kt0", "kt1"):
                    m, free = filled(name, b)
                    u = int(name[2])
                    dve.tensor_copy(KT[:, q, :, u * P:(u + 1) * P],
                                    flat(m).rearrange("p (a s) -> p a s", a=4)).then_inc(free, 1)

            def post(name, b):
                q, z = b % 2, b % 3
                if name == "oa":
                    dve.wait_ge(s_exp, NH * (b + 1))
                    link(dve.reciprocal(rinv[:, :, :], rsum[:, q, :, :]))
                    dve.wait_ge(s_pv, NH * (b + 1))
                    if b:
                        dve.wait_ge(s_mp, number["ot", b - 1] + 1)
                    dve.tensor_tensor(Oa[:, :, :].rearrange("p u (h d) -> p u h d", h=NH),
                                      PO[q][:, :, :].rearrange("p u (h d) -> p u h d", h=NH),
                                      rinv[:, :, :].rearrange("p h u -> p u h").unsqueeze(3).to_broadcast([P, 2, NH, DK]),
                                      ALU.mult).then_inc(s_oa, 1)
                elif name == "y":
                    m, free = filled(name, b)
                    dve.tensor_tensor(Z[:, z, :, :], Z[:, z, :, :], m[:, :, :], ALU.add).then_inc(free, 1)
                elif name == "hn":
                    dve.wait_ge(s_r3, b + 1)
                    if b >= 2:
                        dve.wait_ge(s_sct[q], 64 * (b // 2))
                    for u in range(2):
                        last = dve.scalar_tensor_tensor(ROW[:, q, u, 0:D], Z[:, z, u, :], r3[:, u:u + 1], n2w[:, :], ALU.mult, ALU.mult)
                    last.then_inc(s_hn, 1)
                elif name == "lg":
                    m, free = filled(name, b)
                    bc = lambda t: t.unsqueeze(2).to_broadcast([P, 2, NE])
                    d8 = down8[:, :].unsqueeze(1).to_broadcast([P, 2, NE])
                    l3 = m[:, 0, 0:2 * NE].rearrange("p (u e) -> p u e", u=2)
                    ins = dve.tensor_tensor(lg[:, :, :], l3, rbias[:, :].unsqueeze(1).to_broadcast([P, 2, NE]), ALU.add)
                    ins.then_inc(free, 1)
                    read_out(dve, "lg", b)
                    for k, (src, one) in enumerate(((lg, oh1), (lg2, oh2))):
                        link(dve.tensor_reduce(m12[:, :, k], src[:, :, :], AX, ALU.max))
                        link(dve.tensor_tensor(eq[:, :, :], src[:, :, :], bc(m12[:, :, k]), ALU.is_equal))
                        link(dve.tensor_tensor(eq[:, :, :], eq[:, :, :], d8, ALU.mult))
                        link(dve.tensor_reduce(wm[:, :], eq[:, :, :], AX, ALU.max))
                        link(dve.tensor_tensor(one[:, :, :], eq[:, :, :], bc(wm[:, :]), ALU.is_equal))
                        if k == 0:
                            dve.tensor_scalar(ROW[:, q, :, D + 1], wm[:, :], -1.0, float(NE), ALU.mult, ALU.add)
                            link(dve.scalar_tensor_tensor(lg2[:, :, :].rearrange("p u e -> p (u e)"), oh1[:, :, :].rearrange("p u e -> p (u e)"), -3e38,
                                                          lg[:, :, :].rearrange("p u e -> p (u e)"), ALU.mult, ALU.add))
                    dve.tensor_tensor(oh[:, :, :], oh1[:, :, :], oh2[:, :, :], ALU.add).then_inc(s_oh, 1)
                    dve.tensor_tensor(ed[:, :], m12[:, :, 1], m12[:, :, 0], ALU.subtract).then_inc(s_lg, 1)
                elif name == "weights":
                    dve.wait_ge(s_ed, b + 1)
                    link(dve.tensor_scalar(dn[:, :], ed[:, :], 1.0, None, ALU.add))
                    link(dve.reciprocal(dn[:, :], dn[:, :]))
                    link(dve.tensor_tensor(ROW[:, q, :, D + 3], ed[:, :], dn[:, :], ALU.mult))
                    dve.tensor_tensor(ROW[:, q, :, D + 2], dn[:, :], ROW[:, q, :, D + 3], ALU.subtract)
                    dve.tensor_copy(ROW[:, q, :, D], idf[:, 2 * b:2 * b + 2])
                elif name == "rk":
                    m, free = filled(name, b)
                    link(dve.tensor_tensor(pose[:, :, :], m[:, 0, 0:2 * NE].rearrange("p (u e) -> p u e", u=2),
                                           cntE[:, :].unsqueeze(1).to_broadcast([P, 2, NE]), ALU.add))
                    dve.tensor_tensor(cntE[:, :], m[:, 0, 2 * NE:3 * NE], cntE[:, :], ALU.add).then_inc(free, 1)
                    read_out(dve, "rk", b)
                    for k, one in enumerate((oh1, oh2)):
                        link(dve.tensor_tensor(eq[:, :, :], pose[:, :, :], one[:, :, :], ALU.mult))
                        link(dve.tensor_reduce(posf[:, :, k], eq[:, :, :], AX, ALU.add))
                    dve.tensor_copy(pos[:, q, :, :], posf[:, :, :]).then_inc(s_pos, 1)

            def maxima(g):
                q, h, r = (g // NH) % 2, g % NH, g % NR
                dve.wait_ge(s_sc, g + 1)
                if g >= NR:
                    dve.wait_ge(s_exp, g - NR + 1)
                f = flat(SC[g % 2])
                dve.tensor_tensor_reduce(Sm[:, r, 0:P], f[:, 0:P], mask[:, 0:P], -(DK ** -0.5), 3e38, ALU.add, ALU.min,
                                         nm[:, q, h, 0:1])
                dve.tensor_tensor_reduce(Sm[:, r, P:3 * P], f[:, P:3 * P], mask[:, P:3 * P], -(DK ** -0.5), 3e38, ALU.add, ALU.min,
                                         nm[:, q, h, 1:2]).then_inc(s_mx, 1)

            def evac(g):
                dve.wait_ge(s_ptp, g + 1)
                if g >= NR:
                    dve.wait_ge(s_pv, g - NR + 1)
                dve.tensor_copy(PTs[:, g % NR, :], flat(PTp[g % 2])[:, 0:3 * P]).then_inc(s_pte[g % 2], 1)

            norms(0)
            for name in PREP:
                prep(name, 0)
            for b in range(B + 1):
                for h in range(NH):
                    g = b * NH + h
                    if h == 0 and b + 1 < B:
                        norms(b + 1)
                    if g % 2 == 0 and 3 <= g < B * NH + 3:
                        evac(g - 3)
                    if h == 5 and b >= 1:
                        post("oa", b - 1)
                    if g < B * NH:
                        maxima(g)
                    if h in LATE_PREP and b + 1 < B:
                        prep(LATE_PREP[h], b + 1)
                    if h in LATE_POST and b >= 1:
                        post(LATE_POST[h], b - 1)
                    if h in AT_PREP and AT_PREP[h][0] != "q" or h in AT_PREP and AT_PREP[h][1] == "t":
                        if b + 1 < B:
                            prep(AT_PREP[h], b + 1)
                    if h in AT_POST and b >= 1:
                        post(AT_POST[h], b - 1)

            link(dve.tensor_tensor(fcum[:, :], cntE[0:1, :], ecap[0:1, :], ALU.subtract))
            link(dve.tensor_copy(regs[0:1, 0:NE], fcum[:, :]))
            link(dve.tensor_scalar(fcum[:, :], fcum[:, :], 1.0, float(GT - 1), ALU.max, ALU.add))
            link(dve.tensor_copy(icnt[:, :], fcum[:, :]))
            link(dve.tensor_scalar(icnt[:, :], icnt[:, :], 8, None, ALU.arith_shift_right))
            link(dve.tensor_copy(fcum[:, :], icnt[:, :]))
            link(dve.tensor_tensor_scan(fcum[:, :], fcum[:, :], ones[0:1, 0:NE], 0.0, ALU.add, ALU.mult))
            dve.tensor_copy(regs[0:1, NE:2 * NE], fcum[:, :]).then_inc(s_regs, 1)
            dve.sem_inc(s_mt, 1)
            dve.sem_inc(s_xsT, 1)
            dve.sem_inc(s_hb, 3)
            dve.sem_inc(s_yf, 1)
            dve.sem_inc(s_added, 1)
            dve.wait_ge(s_bout, 16 * (B + 1))
            dve.wait_ge(s_b, 48)
            dve.wait_ge(s_regs, 1)
            cum = [0] + [dve.value_load(regs[0:1, NE + e:NE + e + 1], min_val=e + 1, max_val=8 * (e + 1)) for e in range(NE)]
            dve.wait_ge(s_xs, 16)
            dve.tensor_copy(MN[:, :, :], XS[:, :, D:RW]).then_inc(s_mt, 1)
            dve.wait_ge(s_xh, 1)
            dve.tensor_tensor(xsL, XB[:, :, :], xsH.bitcast(fp32), ALU.subtract).then_inc(s_xsT, 1)
            for e in range(NE):
                with dve.Fori(cum[e], cum[e + 1]) as i:
                    dve.wait_ge(s_mt, i + 2)
                    dve.tensor_copy(MT[:, :, :], MN[:, :, :]).then_inc(s_mm, 1)
                    for f in range(FC):
                        dve.wait_ge(s_silu, i * FC + f + 1)
                        dve.scalar_tensor_tensor(htmp[:, f % 2, :], HB[f % 3][:, 1, :], b2T[:, e, f:f + 1], silu[:, f % 2, :],
                                                 ALU.add, ALU.mult).then_inc(s_hb, 1)
                        dve.wait_ge(s_hb, i * FC + f + 4)
                        dve.tensor_copy(hH[:, f, :], htmp[:, f % 2, :]).then_inc(s_hi, 1)
                        dve.wait_ge(s_hi, i * FC + f + 1)
                        dve.tensor_tensor(hL[:, f, :], htmp[:, f % 2, :], hH[:, f, :].bitcast(fp32), ALU.subtract).then_inc(s_hl, 1)
                    dve.wait_ge(s_xs, i * 16 + 32)
                    dve.wait_ge(s_mm, i + 1)
                    dve.tensor_copy(MN[:, :, :], XS[:, :, D:RW]).then_inc(s_mt, 1)
                    dve.wait_ge(s_xh, i + 2)
                    dve.tensor_tensor(xsL, XB[:, :, :], xsH.bitcast(fp32), ALU.subtract).then_inc(s_xsT, 1)
                    dve.wait_ge(s_added, i + 1)
                    dve.tensor_copy(ids[:, :], MT[:, :, 0])
                    dve.tensor_scalar(wrow[:, :], MT[:, :, 1], float(e), None, ALU.is_equal).then_inc(s_wr, 1)
                    dve.wait_ge(s_wr, i * 3 + 1)
                    dve.tensor_tensor(wrow[:, :], wrow[:, :], MT[:, :, 2], ALU.mult).then_inc(s_wr, 1)
                    dve.wait_ge(s_wr, i * 3 + 2)
                    dve.tensor_tensor(wrow[:, :], wrow[:, :], MT[:, :, 3], ALU.add).then_inc(s_wr, 1)
                    dve.wait_ge(s_it, i + 1)
                    for u in range(2):
                        last = dve.tensor_tensor(Yt[:, u, :], YB[u][:, 0, :], b3b[:, e, :], ALU.add)
                    last.then_inc(s_yf, 1)
                    dve.wait_ge(s_yf, i + 2)
                    dve.wait_ge(s_wr, i * 3 + 3)
                    for u in range(2):
                        last = dve.tensor_scalar(Yb[:, u, :], Yt[:, u, :], wrow[:, u:u + 1], None, ALU.mult)
                    last.then_inc(s_y, 1)


def kernel(**inputs):
    import numpy as np
    import concourse.bacc as bacc
    from concourse.bass_utils import run_bass_kernel_spmd as run

    nc = bacc.Bacc("TRN2", target_bir_lowering=False, num_devices=1)
    arrays, A = {}, {}

    def give(name, a):
        a = np.ascontiguousarray(a)
        arrays[f"in_{name}"] = a
        A[name] = nc.dram_tensor(f"in_{name}", a.shape, mybir.dt.from_np(a.dtype), kind="ExternalInput").ap()

    for name in ("x", "ctx_1024"):
        give(name, inputs[name])
    for name in ("norm1_w", "Wq", "Wk", "Wv", "Wo", "norm2_w", "router_w", "router_b", "W1", "b1", "W2", "b2", "W3", "b3"):
        give(name, inputs[f"L0_ffn_{name}"])
    half = D // 2
    theta = (1.0 / np.float32(10000.0) ** (np.arange(half, dtype=np.float32) / np.float32(half))).astype(np.float32)
    angle = np.arange(S, dtype=np.float32)[:, None] * theta[None, :]
    give("cos", np.cos(angle).astype(np.float32))
    give("sin", np.sin(angle).astype(np.float32))
    corner = np.full((P, 1), BIG, np.float32)
    corner[NC - 1::LANES] = 0.0
    give("corner", corner)
    out = nc.dram_tensor("out", (B * S + GT, D), mybir.dt.float32, kind="ExternalOutput").ap()
    xattn_moe_kernel(nc, A, out)
    r = run(nc, [arrays], core_ids=[0])
    return r.results[0]["out"][0:B * S].reshape(B, S, D)
```
